# Optimizing a Trainium2 kernel written in Bass

```python
import numpy as np
import jax
import jax.numpy as jnp

def _softmax(x, axis=-1):
    return jax.nn.softmax(x, axis=axis)
def _gelu(x):
    return jax.nn.gelu(x, approximate=True)
def _silu(x):
    return jax.nn.silu(x)
def _sigmoid(x):
    return jax.nn.sigmoid(x)
def _layernorm(x, axis=-1, eps=1e-5):
    m = jnp.mean(x, axis=axis, keepdims=True)
    v = jnp.var(x, axis=axis, keepdims=True)
    return (x - m) / jnp.sqrt(v + eps)
def _scatter_add(tgt, idx, src, axis=0):
    return tgt.at[idx].add(src)
def _segment_sum(src, seg, n):
    return jax.ops.segment_sum(src, seg, n)

kernel_name = 'mk_adj_preln_d1_adj_1024_567e30'

def setup_inputs(seed: int = 0):
    np.random.seed(seed)
    _w = jnp.asarray
    def _rec_inputs():
        import jax
        import jax.numpy as jnp
        _gk = jax.random.key(seed)
        x = -0.0003929 + 0.9999 * jax.random.normal(jax.random.fold_in(_gk, 1), (32, 512, 1024), jnp.float32)
        _a = jax.random.bernoulli(jax.random.fold_in(_gk, 2), 0.0625, (512, 512))
        _a = jnp.logical_or(_a, jnp.swapaxes(_a, -1, -2))
        _a = jnp.logical_or(_a, jnp.eye(512, dtype=bool))
        _af = _a.astype(jnp.float32)
        _af = _af * jax.random.uniform(jax.random.fold_in(_gk, 3), (512, 512), jnp.float32, 0.05, 0.198159)
        adj = _af
        return x, adj
    x, adj = _rec_inputs()
    def _L0_gnn_setup():
        import jax, jax.numpy as jnp
        import numpy as np
        NEG_SLOPE = 0.01
        key = jax.random.key(seed)
        k1, k2, k3, k4, k5 = jax.random.split(key, 5)
        B, C, N, O = (32, 512, 1024, 512)
        x = jax.random.normal(k1, (B, C, N), dtype=jnp.float32)
        wq = jax.random.normal(k2, (C,), dtype=jnp.float32) * (1.0 / np.sqrt(C))
        wk = jax.random.normal(k3, (C,), dtype=jnp.float32) * (1.0 / np.sqrt(C))
        wm = jax.random.normal(k4, (O, C), dtype=jnp.float32) * (1.0 / np.sqrt(C))
        bm = jax.random.normal(k5, (O,), dtype=jnp.float32) * 0.01
        return {'x': x, 'wq': wq, 'wk': wk, 'wm': wm, 'bm': bm}
    _L0_gnn_all = _L0_gnn_setup()
    _L0_gnn_in = {k: v for k, v in _L0_gnn_all.items() if k in ('wq', 'wk', 'bm', )}
    del _L0_gnn_all

    return {
        "x": x,
        "adj": adj,
        "L0_gnn_wq": _L0_gnn_in["wq"],
        "L0_gnn_wk": _L0_gnn_in["wk"],
        "L0_gnn_bm": _L0_gnn_in["bm"],
    }

def reference(x, adj, L0_gnn_wq, L0_gnn_wk, L0_gnn_bm):
    import jax
    import jax.numpy as jnp
    def _L0_gnn_ref(x, wq, wk, wm, bm):
        import jax, jax.numpy as jnp
        import numpy as np
        NEG_SLOPE = 0.01
        q = jnp.einsum('c,bcn->bn', wq, x)
        k = jnp.einsum('c,bcn->bn', wk, x)
        scores = q[:, None, :] + k[:, :, None]
        scores = jnp.where(scores > 0, scores, NEG_SLOPE * scores)
        att = jax.nn.softmax(scores, axis=-1)
        agg = jnp.einsum('bcn,bmn->bcm', x, att)
        out = jnp.einsum('oc,bcm->bom', wm, agg) + bm[None, :, None]
        return jax.nn.relu(out)

    h = jnp.maximum(_layernorm(x, axis=-1), 0.0)
    x = x + _L0_gnn_ref(h, L0_gnn_wq, L0_gnn_wk, adj, L0_gnn_bm)
    return x


_drawn_inputs = setup_inputs


def setup_inputs(seed=0):
    import zlib

    import numpy as np

    out = dict(_drawn_inputs(seed))
    spreads = {}
    factors = {'L0_gnn_wq': 8.0, 'L0_gnn_wk': 8.0, 'L0_gnn_bm': 8.0}
    for name, (base, spread) in spreads.items():
        noise = np.random.default_rng([zlib.crc32(name.encode()), seed]).standard_normal(out[name].shape)
        drawn = base * np.exp(spread * noise) if base else spread * noise
        out[name] = jnp.asarray(drawn.astype(out[name].dtype))
    for name, factor in factors.items():
        out[name] = (out[name] * factor).astype(out[name].dtype)
    return out
```

```python
import concourse.bass as bass
from concourse import mybir
from contextlib import ExitStack


def preln_graph_attention_kernel(
    nc: bass.Bass,
    x: bass.AP,
    adj: bass.AP,
    wq: bass.AP,
    wk: bass.AP,
    bm: bass.AP,
    out: bass.AP,
):
    f32, f16, bf16, u32 = mybir.dt.float32, mybir.dt.float16, mybir.dt.bfloat16, mybir.dt.uint32
    ALU = mybir.AluOpType
    ACT = mybir.ActivationFunctionType
    AX = mybir.AxisListType

    NB, C, N = x.shape
    O = adj.shape[0]
    P = 128
    CT, OT, NT = C // P, O // P, N // P
    MH = 512
    HALVES = N // MH
    GROUPS = HALVES * OT
    XS = 3
    OB = 4
    WC = O + 2
    WB = WC // 2
    EPS = 1e-5
    SLOPE = 0.01
    ATT_SCALE = 2.0 ** 15
    Z_CAP = 80.0
    MIN_SCALE = 2.0 ** -120
    EXPONENT_BITS = 0x7F800000

    q_dram = nc.dram_tensor("q_row", [N], f32).ap()
    ab_dram = nc.dram_tensor("ab_rows", [2, N], f32).ap()

    ctx = ExitStack()
    with ctx:
        def sb(name, shape, dt):
            return ctx.enter_context(nc.sbuf_tensor(name, shape, dt))

        def sem(name):
            return ctx.enter_context(nc.semaphore(name))

        x_sb = sb("x_sb", [P, XS, CT, N], f32)
        h_sb = sb("h_sb", [P, 2, CT, N], f16)
        y_sb = sb("y_sb", [P, 2, 2, NT, WC], f16)
        att_sb = sb("att_sb", [P, 2, HALVES, 2, NT, MH], f16)
        w_sb = sb("w_sb", [P, 2, CT, WC], f16)
        rows = sb("rows", [P, 2, N], f32)
        xn = sb("xn", [P, 2, N], f32)
        att_a = sb("att_a", [P, 2, MH], f32)
        att_f = sb("att_f", [P, 2, MH], f32)
        relu_out = sb("relu_out", [P, 2, MH], f32)
        unused = sb("unused", [P, 2, N], bf16)
        stats = sb("stats", [P, CT, 2, 6], f32)
        mean_var = sb("mean_var", [P, CT, 2], f32)
        var_eps = sb("var_eps", [P, CT], f32)
        minus_half = sb("minus_half", [P, CT], f32)
        three_halves = sb("three_halves", [P, CT], f32)
        eps = sb("eps", [P, CT], f32)
        rs0 = sb("rs0", [P, CT], f32)
        rs1 = sb("rs1", [P, CT], f32)
        rs2 = sb("rs2", [P, CT], f32)
        rs3 = sb("rs3", [P, CT], f32)
        rstd = sb("rstd", [P, CT], f32)
        qk_col = sb("qk_col", [P, 2, NT], f32)
        qmax = sb("qmax", [P, 3], f32)
        z_col = sb("z_col", [P, 2, NT], f32)
        r_col = sb("r_col", [P, NT], f32)
        e_col = sb("e_col", [P, 2, NT], f32)
        den = sb("den", [P, NT], f32)
        rden = sb("rden", [P, NT], f32)
        ab_col = sb("ab_col", [P, 2, NT], f32)
        bias = sb("bias", [P, OT], f32)
        out_scale = sb("out_scale", [P, OT], f32)
        qk_scale = sb("qk_scale", [P, 2], f32)
        prep = att_sb[:, :, :, :, :, :].rearrange("p a b c d e -> p (a b c d e)").bitcast(f32)
        adj_f = prep[:, 0:OT * C].rearrange("p (o c) -> p o c", o=OT)
        adj_s = prep[:, OT * C:2 * OT * C].rearrange("p (o c) -> p o c", o=OT)
        qk_all = prep[:, 2 * OT * C:2 * OT * C + 2 * C].rearrange("p (j c) -> p j c", j=2)
        at = 2 * OT * C + 2 * C
        ident = prep[:, at:at + P]
        qk_w = prep[:, at + P:at + P + 2 * CT].rearrange("p (j c) -> p j c", j=2)
        qk_ws = prep[:, at + P + 8:at + P + 8 + 2 * CT].rearrange("p (j c) -> p j c", j=2)
        amax = prep[:, at + P + 16:at + P + 22]
        amax_g = prep[:, at + P + 24:at + P + 30]
        pow2 = prep[:, at + P + 32:at + P + 38]
        inv2 = prep[:, at + P + 40:at + P + 46]

        psY = ctx.enter_context(nc.psum_tensor("psY", [P, 2, 2, 512], f32))
        psO = ctx.enter_context(nc.psum_tensor("psO", [P, OB, MH], f32))

        x_loaded = [[sem(f"x_loaded{o}_{p}") for p in range(2)] for o in range(CT)]
        x_stored = [sem(f"x_stored{o}") for o in range(OT)]
        s_w = sem("weights_loaded")
        s_prep = sem("prep_step")
        s_ident = sem("ident_ready")
        s_const = sem("const_ready")
        s_wT = sem("adj_transposed")
        s_whi = sem("w_hi_ready")
        s_w_ready = sem("w_ready")
        s_stats = sem("stats_ready")
        s_mv = sem("mean_var_ready")
        s_rs = sem("rstd_step")
        s_rstd = sem("rstd_ready")
        s_xn = sem("xn_ready")
        s_hhi = sem("h_hi_ready")
        s_h = sem("h_ready")
        s_ydone = sem("y_done")
        s_yhi = sem("y_hi_ready")
        s_y = sem("y_ready")
        s_qk = sem("qk_ready")
        s_qout = sem("q_in_dram")
        s_qbc = sem("q_spread")
        s_qmax = sem("qmax_step")
        s_z = sem("z_step")
        s_e = sem("e_ready")
        s_den = sem("den_ready")
        s_rden = sem("rden_ready")
        s_ab = sem("ab_ready")
        s_about = sem("ab_in_dram")
        s_abbc = sem("ab_spread")
        s_a = sem("att_a_ready")
        s_af = sem("att_f_ready")
        s_ahi = sem("att_hi_ready")
        s_att = sem("att_ready")
        s_odone = sem("out_done")
        s_relu = sem("out_bank_free")
        s_added = sem("relu_out_free")

        block = ctx.enter_context(nc.Block())

        def slots(eng, slot):
            slot(-1, 1)
            with eng.Fori(0, (NB - 2) // 2) as i:
                for par in range(2):
                    slot(eng.snap(2 * i + par), par)
            slot(NB - 2, 0)
            slot(NB - 1, 1)

        def last(s):
            return NB - 1 - s if isinstance(s, int) else 2

        def x_tile(eng, b, o, lo=0, hi=N):
            if isinstance(b, int):
                return x_sb[:, b % XS, o, lo:hi]
            return x_sb[:, bass.ds(b, 1), o, lo:hi]

        def x_slot(eng, b):
            return b if isinstance(b, int) else eng.snap(b % XS)

        @block.sync
        def _(sp):
            sp.dma_start(adj_f, adj.rearrange("(t p) c -> p t c", p=P)).then_inc(s_w, 16)
            for j, w in enumerate((wq, wk)):
                sp.dma_start(qk_all[:, j, :], w.rearrange("(a c) -> a c", a=1).broadcast_to([P, C])).then_inc(s_w, 16)

            def load_x(b, par, need_store):
                for o in range(CT):
                    if need_store is not None:
                        sp.wait_ge(x_stored[o], need_store)
                    src = x[b, o * P:(o + 1) * P, :] if isinstance(b, int) else \
                        x[bass.ds(b, 1), o * P:(o + 1) * P, :].rearrange("b p n -> p b n")
                    sp.dma_start(x_tile(sp, x_slot(sp, b), o), src).then_inc(x_loaded[o][par], 16)

            for o in range(OT):
                sp.sem_inc(x_stored[o], 16)
            load_x(0, 0, None)
            load_x(1, 1, None)

            def slot(s, par):
                if last(s) >= 2 and not (isinstance(s, int) and s < 0):
                    load_x(s + 2, par, s * 16 + 16)
                if last(s) >= 1:
                    sp.wait_ge(s_qk, s + 2)
                    sp.dma_start(q_dram.rearrange("(p t) -> p t", t=NT), qk_col[:, 0, :]).then_inc(s_qout, 16)
                    sp.wait_ge(s_qout, (s + 2) * 16)
                    if not (isinstance(s, int) and s < 0):
                        sp.wait_ge(s_att, (s + 1) * 2 * NT)
                    sp.dma_start(rows[:, 0, :], q_dram.rearrange("(a n) -> a n", a=1).broadcast_to([P, N]))\
                      .then_inc(s_qbc, 16)
                    sp.wait_ge(s_ab, s + 2)
                    sp.dma_start(ab_dram.rearrange("j (p t) -> p j t", t=NT), ab_col[:, :, :]).then_inc(s_about, 16)
                    sp.wait_ge(s_about, (s + 2) * 16)
                    sp.dma_start(rows[:, :, :],
                                 ab_dram.rearrange("(a j) n -> a j n", a=1).broadcast_to([P, 2, N]))\
                      .then_inc(s_abbc, 16)
                if not (isinstance(s, int) and s < 0):
                    xs = x_slot(sp, s)
                    for o in range(OT):
                        sp.wait_ge(s_added, s * GROUPS + (2 + GROUPS - OT + o + 1))
                        dst = out[s, o * P:(o + 1) * P, :] if isinstance(s, int) else \
                            out[bass.ds(s, 1), o * P:(o + 1) * P, :].rearrange("b p n -> p b n")
                        sp.dma_start(dst, x_tile(sp, xs, o)).then_inc(x_stored[o], 16)

            slots(sp, slot)
            for o in range(OT):
                sp.wait_ge(x_stored[o], 16 * (NB + 1))

        @block.gpsimd
        def _(pool):
            nc.gpsimd.memset(ident, 0.0).then_inc(s_ident, 1)
            nc.gpsimd.memset(minus_half[:, :], -0.5)
            nc.gpsimd.memset(three_halves[:, :], 1.5)
            nc.gpsimd.memset(eps[:, :], EPS).then_inc(s_const, 1)
            nc.gpsimd.memset(relu_out[:, 0, :], 0.0).then_inc(s_added, 1)
            nc.gpsimd.memset(relu_out[:, 1, :], 0.0).then_inc(s_added, 1)
            pool.wait_ge(s_ident, 1)
            nc.gpsimd.affine_select(out=ident, in_=ident, compare_op=ALU.not_equal, fill=1.0, base=0,
                                    pattern=[[-1, P]], channel_multiplier=1).then_inc(s_ident, 1)
            pool.wait_ge(s_const, 1)

            def inverse_root(b):
                pool.wait_ge(s_mv, b + 1)
                nc.gpsimd.tensor_tensor(var_eps[:, :], mean_var[:, :, 1], eps[:, :], ALU.add).then_inc(s_rs, 1)
                pool.wait_ge(s_rs, b * 6 + 1)
                nc.gpsimd.tensor_tensor(rs0[:, :], var_eps[:, :], minus_half[:, :], ALU.pow).then_inc(s_rs, 1)
                pool.wait_ge(s_rs, b * 6 + 2)
                nc.gpsimd.tensor_tensor(rs1[:, :], var_eps[:, :], rs0[:, :], ALU.mult).then_inc(s_rs, 1)
                pool.wait_ge(s_rs, b * 6 + 3)
                nc.gpsimd.tensor_tensor(rs2[:, :], rs1[:, :], rs0[:, :], ALU.mult).then_inc(s_rs, 1)
                pool.wait_ge(s_rs, b * 6 + 4)
                nc.gpsimd.tensor_tensor(rs3[:, :], rs2[:, :], minus_half[:, :], ALU.mult).then_inc(s_rs, 1)
                pool.wait_ge(s_rs, b * 6 + 5)
                nc.gpsimd.tensor_tensor(rs1[:, :], rs3[:, :], three_halves[:, :], ALU.add).then_inc(s_rs, 1)
                pool.wait_ge(s_rs, b * 6 + 6)
                nc.gpsimd.tensor_tensor(rstd[:, :], rs1[:, :], rs0[:, :], ALU.mult).then_inc(s_rstd, 1)

            inverse_root(0)

            def slot(s, par):
                if last(s) >= 2:
                    inverse_root(s + 2)
                if isinstance(s, int) and s < 0:
                    return
                xs = x_slot(pool, s)
                for g in range(GROUPS):
                    half, o = divmod(g, OT)
                    pool.wait_ge(s_relu, s * GROUPS + (CT + g + 1))
                    xt = x_tile(pool, xs, o, half * MH, (half + 1) * MH)
                    nc.gpsimd.tensor_tensor(xt, xt, relu_out[:, g % 2, :], ALU.add).then_inc(s_added, 1)

            slots(pool, slot)

        @block.scalar
        def _(act):
            act.dma_start(bias[:, :], bm.rearrange("(t p) -> p t", p=P), allow_slow_non_contiguous=True).then_inc(s_w, 16)
            for j, w in enumerate((wq, wk)):
                act.dma_start(qk_w[:, j, :], w.rearrange("(t p) -> p t", p=P), allow_slow_non_contiguous=True)\
                   .then_inc(s_w, 16)
            for c in range(CT):
                act.wait_ge(s_wT, c + 1)
                nc.scalar.activation(w_sb[:, 0, c, 0:O], psO[:, c, :], ACT.Copy).then_inc(s_whi, 1)

            def h_hi(b, o):
                act.wait_ge(s_xn, b * CT + (o + 1))
                nc.scalar.activation(h_sb[:, 0, o, :], xn[:, o % 2, :], ACT.Relu).then_inc(s_hhi, 1)

            def exps(b):
                act.wait_ge(s_z, b * 2 + 2)
                nc.scalar.activation(r_col[:, :], z_col[:, 1, :], ACT.Exp)
                nc.scalar.activation(e_col[:, 0, :], qk_col[:, 0, :], ACT.Exp, bias=qmax[:, 1:2])
                nc.scalar.activation(e_col[:, 1, :], qk_col[:, 0, :], ACT.Exp, bias=qmax[:, 2:3], scale=SLOPE)
                nc.scalar.activation(rows[:, 1, :], rows[:, 0, :], ACT.Exp, bias=qmax[:, 2:3], scale=SLOPE)
                nc.scalar.activation(rows[:, 0, :], rows[:, 0, :], ACT.Exp, bias=qmax[:, 1:2]).then_inc(s_e, 1)

            def a_part(b, half, t):
                i = half * NT + t
                if isinstance(b, int) and b == 0 and i < 2:
                    pass
                else:
                    act.wait_ge(s_af, b * 2 * NT + (i - 1))
                if t == 0:
                    act.wait_ge(s_abbc, b * 16 + 16)
                nc.scalar.activation(att_a[:, i % 2, :], rows[:, 0, half * MH:(half + 1) * MH], ACT.Copy,
                                     scale=e_col[:, 0, t:t + 1]).then_inc(s_a, 1)

            def att_hi(b, par, half, t):
                i = half * NT + t
                act.wait_ge(s_af, b * 2 * NT + (i + 1))
                nc.scalar.activation(att_sb[:, par, half, 0, t, :], att_f[:, i % 2, :], ACT.Copy)\
                  .then_inc(s_ahi, 1)

            def y_hi(b, par, t):
                act.wait_ge(s_ydone, b * NT + (t + 1))
                nc.scalar.activation(y_sb[:, par, 0, t, :].rearrange("p (j c) -> p j c", j=2),
                                     psY[:, t % 2, :, 0:WB], ACT.Copy).then_inc(s_yhi, 1)

            def relu(s, g):
                act.wait_ge(s_odone, s * GROUPS + (g + 1))
                act.wait_ge(s_added, s * GROUPS + (g + 1))
                nc.scalar.activation(relu_out[:, g % 2, :], psO[:, g % OB, :], ACT.Relu,
                                     bias=bias[:, g % OT:g % OT + 1],
                                     scale=out_scale[:, g % OT:g % OT + 1]).then_inc(s_relu, 1)

            for o in range(CT):
                h_hi(0, o)

            def slot(s, par):
                first = isinstance(s, int) and s < 0
                for t in range(0, NT, 2):
                    if not first:
                        a_part(s, 1, t)
                        a_part(s, 1, t + 1)
                        att_hi(s, par, 1, t)
                    if last(s) >= 1:
                        y_hi(s + 1, 1 - par, t)
                    if not first:
                        att_hi(s, par, 1, t + 1)
                    if last(s) >= 1:
                        y_hi(s + 1, 1 - par, t + 1)
                if last(s) >= 1:
                    exps(s + 1)
                if not first:
                    for g in range(3):
                        relu(s, g)
                if last(s) >= 2:
                    for o in range(CT):
                        h_hi(s + 2, o)
                if not first:
                    for g in range(3, 5):
                        relu(s, g)
                if last(s) >= 1:
                    for t in range(0, NT, 2):
                        a_part(s + 1, 0, t)
                        a_part(s + 1, 0, t + 1)
                        att_hi(s + 1, 1 - par, 0, t)
                        att_hi(s + 1, 1 - par, 0, t + 1)
                        if t == 4 and not first:
                            relu(s, 5)
                elif not first:
                    relu(s, 5)
                if not first:
                    relu(s, 6)
                    relu(s, 7)

            slots(act, slot)

        @block.vector
        def _(dve):
            dve.wait_ge(s_w, 16 * 6)
            for o in range(OT):
                nc.vector.reduce_max(amax[:, o:o + 1], adj_f[:, o, :], AX.X, apply_absolute_value=True)
            for j in range(2):
                step = nc.vector.reduce_max(amax[:, OT + j:OT + j + 1], qk_all[:, j, :], AX.X,
                                            apply_absolute_value=True)
            step.then_inc(s_prep, 1)
            dve.wait_ge(s_prep, 1)
            nc.vector.tensor_scalar(amax_g, amax, MIN_SCALE, None, ALU.max).then_inc(s_prep, 1)
            dve.wait_ge(s_prep, 2)
            nc.vector.tensor_scalar(pow2.bitcast(u32), amax_g.bitcast(u32), EXPONENT_BITS, None,
                                    ALU.bitwise_and).then_inc(s_prep, 1)
            dve.wait_ge(s_prep, 3)
            nc.vector.reciprocal(inv2, pow2).then_inc(s_prep, 1)
            nc.vector.tensor_scalar(out_scale[:, :], pow2[:, 0:OT], 1.0 / ATT_SCALE, None, ALU.mult)
            nc.vector.tensor_copy(qk_scale[:, :], pow2[:, OT:OT + 2])
            dve.wait_ge(s_prep, 4)
            for o in range(OT):
                nc.vector.tensor_scalar(adj_s[:, o, :], adj_f[:, o, :], inv2[:, o:o + 1], None, ALU.mult)
            for j in range(2):
                step = nc.vector.tensor_scalar(qk_ws[:, j, :], qk_w[:, j, :], inv2[:, OT + j:OT + j + 1], None,
                                               ALU.mult)
            step.then_inc(s_prep, 1)
            dve.wait_ge(s_prep, 5)
            nc.vector.tensor_copy(w_sb[:, 0, :, O:WC].rearrange("p c j -> p j c"), qk_ws).then_inc(s_prep, 1)
            dve.wait_ge(s_prep, 6)
            nc.vector.tensor_tensor(w_sb[:, 1, :, O:WC].rearrange("p c j -> p j c"), qk_ws,
                                    w_sb[:, 0, :, O:WC].rearrange("p c j -> p j c"), ALU.subtract)
            for c in range(CT):
                dve.wait_ge(s_whi, c + 1)
                nc.vector.tensor_tensor(w_sb[:, 1, c, 0:O], psO[:, c, :], w_sb[:, 0, c, 0:O], ALU.subtract)\
                  .then_inc(s_relu, 1)

            def layer_stats(b, par):
                xs = x_slot(dve, b)
                for o in range(CT):
                    dve.wait_ge(x_loaded[o][par], b * 8 + (16 - 8 * par))
                    for j in range(2):
                        step = nc.vector.bn_stats(stats[:, o, j, :],
                                                  x_tile(dve, xs, o, j * 512, (j + 1) * 512))
                step.then_inc(s_stats, 1)
                dve.wait_ge(s_stats, b + 1)
                dve.nop(nofuse=True)
                for o in range(CT):
                    step = nc.vector.bn_aggr(mean_var[:, o, :], stats[:, o, :, :].rearrange("p a b -> p (a b)"))
                step.then_inc(s_mv, 1)

            def layer_norm(b):
                xs = x_slot(dve, b)
                dve.wait_ge(s_rstd, b + 1)
                for pair in range(0, CT, 2):
                    for o in (pair, pair + 1):
                        if not (isinstance(b, int) and b == 0 and o < 2):
                            dve.wait_ge(s_h, b * CT + (o - 1))
                        nc.vector.tensor_scalar(xn[:, o % 2, :] if isinstance(b, int) else xn[:, o % 2:o % 2 + 1, :],
                                                x_tile(dve, xs, o), mean_var[:, o, 0:1], rstd[:, o:o + 1],
                                                ALU.subtract, ALU.mult).then_inc(s_xn, 1)
                    for o in (pair, pair + 1):
                        dve.wait_ge(s_hhi, b * CT + (o + 1))
                        nc.vector.scalar_tensor_tensor(h_sb[:, 1, o, :], xn[:, o % 2, :], 0.0,
                                                       h_sb[:, 0, o, :], ALU.max, ALU.subtract)\
                          .then_inc(s_h, 1)

            def att_sum(b, half, t):
                i = half * NT + t
                if t == 0:
                    dve.wait_ge(s_abbc, b * 16 + 16)
                dve.wait_ge(s_a, b * 2 * NT + (i + 1))
                if not (isinstance(b, int) and b == 0 and i < 2):
                    dve.wait_ge(s_att, b * 2 * NT + (i - 1))
                nc.vector.scalar_tensor_tensor(att_f[:, i % 2, :], rows[:, 1, half * MH:(half + 1) * MH],
                                               e_col[:, 1, t:t + 1], att_a[:, i % 2, :], ALU.mult, ALU.max)\
                  .then_inc(s_af, 1)

            def att_lo(b, par, half, t):
                i = half * NT + t
                dve.wait_ge(s_ahi, b * 2 * NT + (i + 1))
                nc.vector.tensor_tensor(att_sb[:, par, half, 1, t, :], att_f[:, i % 2, :],
                                        att_sb[:, par, half, 0, t, :], ALU.subtract).then_inc(s_att, 1)

            def y_lo(b, par, t):
                dve.wait_ge(s_yhi, b * NT + (t + 1))
                step = nc.vector.tensor_tensor(qk_col[:, :, t], psY[:, t % 2, 1, WB - 2:WB], qk_scale[:, :], ALU.mult)
                if t == NT - 1:
                    step.then_inc(s_qk, 1)
                nc.vector.tensor_tensor(y_sb[:, par, 1, t, :].rearrange("p (j c) -> p j c", j=2),
                                        psY[:, t % 2, :, 0:WB],
                                        y_sb[:, par, 0, t, :].rearrange("p (j c) -> p j c", j=2),
                                        ALU.subtract).then_inc(s_y, 1)

            def q_max(b):
                dve.wait_ge(s_qbc, b * 16 + 16)
                nc.vector.reduce_max(qmax[:, 0:1], rows[:, 0, :], AX.X).then_inc(s_qmax, 1)
                dve.wait_ge(s_qmax, b + 1)
                nc.vector.tensor_scalar(z_col[:, 0, :], qk_col[:, 1, :], qmax[:, 0:1], 1.0 - SLOPE,
                                        ALU.add, ALU.mult).then_inc(s_z, 1)
                nc.vector.tensor_scalar(qmax[:, 1:2], qmax[:, 0:1], -1.0, None, ALU.mult)
                nc.vector.tensor_scalar(qmax[:, 2:3], qmax[:, 0:1], -SLOPE, None, ALU.mult)
                dve.wait_ge(s_z, b * 2 + 1)
                nc.vector.tensor_scalar(z_col[:, 1, :], z_col[:, 0, :], Z_CAP, None, ALU.min).then_inc(s_z, 1)

            def denominators(b):
                dve.wait_ge(s_e, b + 1)
                for t in range(NT):
                    if not (isinstance(b, int) and b == 0 and t < 2):
                        dve.wait_ge(s_den, b * NT + (t - 1))
                    nc.vector.scalar_tensor_tensor(unused[:, t % 2, :], rows[:, 0, :], r_col[:, t:t + 1],
                                                   rows[:, 1, :], ALU.mult, ALU.max,
                                                   accum_out=den[:, t:t + 1]).then_inc(s_den, 1)
                dve.wait_ge(s_den, b * NT + NT)
                nc.vector.reciprocal(rden[:, :], den[:, :]).then_inc(s_rden, 1)
                dve.wait_ge(s_rden, b + 1)
                nc.vector.tensor_scalar(ab_col[:, 1, :], rden[:, :], ATT_SCALE, None, ALU.mult)
                nc.vector.scalar_tensor_tensor(ab_col[:, 0, :], rden[:, :], ATT_SCALE, r_col[:, :],
                                               ALU.mult, ALU.mult).then_inc(s_ab, 1)

            layer_stats(0, 0)
            layer_norm(0)

            def slot(s, par):
                first = isinstance(s, int) and s < 0
                for t in range(0, NT, 2):
                    if not first:
                        att_sum(s, 1, t)
                        att_sum(s, 1, t + 1)
                        att_lo(s, par, 1, t)
                    if last(s) >= 1:
                        y_lo(s + 1, 1 - par, t)
                    if not first:
                        att_lo(s, par, 1, t + 1)
                    if last(s) >= 1:
                        y_lo(s + 1, 1 - par, t + 1)
                if last(s) >= 2:
                    layer_stats(s + 2, par)
                if last(s) >= 1:
                    q_max(s + 1)
                    denominators(s + 1)
                if last(s) >= 2:
                    layer_norm(s + 2)
                if last(s) >= 1:
                    for t in range(0, NT, 2):
                        att_sum(s + 1, 0, t)
                        att_sum(s + 1, 0, t + 1)
                        att_lo(s + 1, 1 - par, 0, t)
                        att_lo(s + 1, 1 - par, 0, t + 1)

            slots(dve, slot)

        @block.tensor
        def _(pe):
            pe.wait_ge(s_ident, 2)
            pe.wait_ge(s_prep, 5)
            for c in range(CT):
                for o in range(OT):
                    step = nc.tensor.transpose(psO[:, c, o * P:(o + 1) * P], adj_s[:, o, c * P:(c + 1) * P], ident)
                step.then_inc(s_wT, 1)
            pe.wait_ge(s_relu, CT)

            def y_gemm(b):
                for t in range(NT):
                    if not (isinstance(b, int) and b == 0 and t < 2):
                        pe.wait_ge(s_y, b * NT + (t - 1))
                    for c in range(CT):
                        if t == 0:
                            pe.wait_ge(s_h, b * CT + (c + 1))
                        for n, (hp, wp) in enumerate(((0, 0), (0, 1), (1, 0))):
                            for j in range(2):
                                step = nc.tensor.matmul(psY[:, t % 2, j, 0:WB], h_sb[:, hp, c, t:N:NT],
                                                        w_sb[:, wp, c, j * WB:(j + 1) * WB],
                                                        start=(c == 0 and n == 0), stop=(c == CT - 1 and n == 2))
                    step.then_inc(s_ydone, 1)

            def out_gemm(s, par):
                for g in range(GROUPS):
                    half, o = divmod(g, OT)
                    pe.wait_ge(s_relu, s * GROUPS + (g + 1))
                    for t in range(NT):
                        if g == 0:
                            pe.wait_ge(s_y, s * NT + (t + 1))
                        if o == 0:
                            pe.wait_ge(s_att, s * 2 * NT + (half * NT + t + 1))
                        for n, (yp, ap) in enumerate(((0, 0), (0, 1), (1, 0))):
                            step = nc.tensor.matmul(psO[:, g % OB, :], y_sb[:, par, yp, t, o * P:(o + 1) * P],
                                                    att_sb[:, par, half, ap, t, :],
                                                    start=(t == 0 and n == 0), stop=(t == NT - 1 and n == 2))
                    step.then_inc(s_odone, 1)

            def slot(s, par):
                if last(s) >= 1:
                    y_gemm(s + 1)
                if not (isinstance(s, int) and s < 0):
                    out_gemm(s, par)

            slots(pe, slot)


_INS = ['x', 'adj', 'L0_gnn_wq', 'L0_gnn_wk', 'L0_gnn_bm']


def kernel(**inputs):
    import numpy as _np
    import concourse.bacc as _bacc
    from concourse import mybir as _mybir
    from concourse.bass_utils import run_bass_kernel_spmd as _run

    nc = _bacc.Bacc("TRN2", target_bir_lowering=False, num_devices=1)
    arrays, args = {}, []
    for name in _INS:
        a = _np.ascontiguousarray(inputs[name])
        arrays[f"in_{name}_dram"] = a
        args.append(nc.dram_tensor(f"in_{name}_dram", a.shape, _mybir.dt.from_np(a.dtype), kind="ExternalInput").ap())
    shape = _np.shape(inputs['x'])
    args.append(nc.dram_tensor("out_0_dram", shape, _mybir.dt.float32, kind="ExternalOutput").ap())
    preln_graph_attention_kernel(nc, *args)
    r = _run(nc, [arrays], core_ids=[0])
    return r.results[0]["out_0_dram"]
```

```python
import concourse.bass as bass
from concourse import mybir
from contextlib import ExitStack


def preln_graph_attention_kernel(
    nc: bass.Bass,
    x: bass.AP,
    adj: bass.AP,
    wq: bass.AP,
    wk: bass.AP,
    bm: bass.AP,
    out: bass.AP,
):
    f32, f16, bf16, u32 = mybir.dt.float32, mybir.dt.float16, mybir.dt.bfloat16, mybir.dt.uint32
    ALU = mybir.AluOpType
    ACT = mybir.ActivationFunctionType
    AX = mybir.AxisListType

    NB, C, N = x.shape
    O = adj.shape[0]
    P = 128
    CT, OT, NT = C // P, O // P, N // P
    MH = 512
    HALVES = N // MH
    GROUPS = HALVES * OT
    XS = 3
    OB = 4
    WC = O + 2
    WB = WC // 2
    EPS = 1e-5
    SLOPE = 0.01
    ATT_SCALE = 2.0 ** 15
    Z_CAP = 80.0
    MIN_SCALE = 2.0 ** -120
    EXPONENT_BITS = 0x7F800000

    q_dram = nc.dram_tensor("q_row", [N], f32).ap()
    ab_dram = nc.dram_tensor("ab_rows", [2, N], f32).ap()

    ctx = ExitStack()
    with ctx:
        def sb(name, shape, dt):
            return ctx.enter_context(nc.sbuf_tensor(name, shape, dt))

        def sem(name):
            return ctx.enter_context(nc.semaphore(name))

        x_sb = sb("x_sb", [P, XS, CT, N], f32)
        h_sb = sb("h_sb", [P, 2, CT, N], f16)
        y_sb = sb("y_sb", [P, 2, 2, NT, WC], f16)
        att_sb = sb("att_sb", [P, 2, 2, NT, N], f16)
        w_sb = sb("w_sb", [P, 2, CT, WC], f16)
        rows = sb("rows", [P, 2, N], f32)
        xn = sb("xn", [P, 2, N], f32)
        att_a = sb("att_a", [P, 2, N], f32)
        att_f = sb("att_f", [P, 2, N], f32)
        unused = sb("unused", [P, 2, N], bf16)
        stats = sb("stats", [P, CT, 2, 6], f32)
        mean_var = sb("mean_var", [P, CT, 2], f32)
        var_eps = sb("var_eps", [P, CT], f32)
        minus_half = sb("minus_half", [P, CT], f32)
        minus_one = sb("minus_one", [P, CT], f32)
        three_halves = sb("three_halves", [P, CT], f32)
        eps = sb("eps", [P, CT], f32)
        rs0 = sb("rs0", [P, CT], f32)
        rs1 = sb("rs1", [P, CT], f32)
        rs2 = sb("rs2", [P, CT], f32)
        rs3 = sb("rs3", [P, CT], f32)
        rstd = sb("rstd", [P, CT], f32)
        shift = sb("shift", [P, CT], f32)
        qk_col = sb("qk_col", [P, 2, 2, NT], f32)
        qmax = sb("qmax", [P, 3], f32)
        z_col = sb("z_col", [P, 2, NT], f32)
        r_col = sb("r_col", [P, NT], f32)
        e_col = sb("e_col", [P, 2, NT], f32)
        den = sb("den", [P, NT], f32)
        rden = sb("rden", [P, NT], f32)
        ab_col = sb("ab_col", [P, 2, NT], f32)
        bias = sb("bias", [P, OT], f32)
        out_scale = sb("out_scale", [P, OT], f32)
        qk_scale = sb("qk_scale", [P, 2], f32)
        prep = att_sb[:, 0, :, :, :].rearrange("p a t m -> p (a t m)").bitcast(f32)
        adj_f = prep[:, 0:OT * C].rearrange("p (o c) -> p o c", o=OT)
        adj_s = prep[:, OT * C:2 * OT * C].rearrange("p (o c) -> p o c", o=OT)
        qk_all = prep[:, 2 * OT * C:2 * OT * C + 2 * C].rearrange("p (j c) -> p j c", j=2)
        at = 2 * OT * C + 2 * C
        ident = prep[:, at:at + P]
        qk_w = prep[:, at + P:at + P + 2 * CT].rearrange("p (j c) -> p j c", j=2)
        qk_ws = prep[:, at + P + 8:at + P + 8 + 2 * CT].rearrange("p (j c) -> p j c", j=2)
        amax = prep[:, at + P + 16:at + P + 22]
        amax_g = prep[:, at + P + 24:at + P + 30]
        pow2 = prep[:, at + P + 32:at + P + 38]
        inv2 = prep[:, at + P + 40:at + P + 46]

        h_one = att_sb[:, 1, :, 0:CT, :]

        psY = ctx.enter_context(nc.psum_tensor("psY", [P, 2, 2, 512], f32))
        psO = ctx.enter_context(nc.psum_tensor("psO", [P, OB, MH], f32))

        x_loaded = [[sem(f"x_loaded{o}_{p}") for p in range(2)] for o in range(CT)]
        x_stored = [sem(f"x_stored{o}") for o in range(OT)]
        s_adj = [sem(f"adj_loaded{o}") for o in range(OT)]
        s_w = sem("vectors_loaded")
        s_bias = sem("bias_loaded")
        s_prep = sem("prep_step")
        s_ident = sem("ident_ready")
        s_const = sem("const_ready")
        s_wT = sem("adj_transposed")
        s_whi = sem("w_hi_ready")
        s_w_ready = sem("w_ready")
        s_stats = sem("stats_ready")
        s_mv = sem("mean_var_ready")
        s_rs = sem("rstd_step")
        s_rstd = sem("rstd_ready")
        s_xn = sem("xn_ready")
        s_hhi = sem("h_hi_ready")
        s_h = sem("h_ready")
        s_ydone = sem("y_done")
        s_yhi = sem("y_hi_ready")
        s_y = sem("y_ready")
        s_qk = sem("qk_ready")
        s_qout = sem("q_in_dram")
        s_qbc = sem("q_spread")
        s_qmax = sem("qmax_step")
        s_z = sem("z_step")
        s_e = sem("e_ready")
        s_den = sem("den_ready")
        s_rden = sem("rden_ready")
        s_ab = sem("ab_ready")
        s_about = sem("ab_in_dram")
        s_abbc = sem("ab_spread")
        s_qk0 = sem("qk_done")
        s_a = sem("att_a_ready")
        s_af = sem("att_f_ready")
        s_ahi = sem("att_hi_ready")
        s_att = sem("att_ready")
        s_odone = sem("out_done")
        s_relu = sem("relu_ready")
        s_added = sem("residual_added")

        block = ctx.enter_context(nc.Block())

        def slots(eng, slot):
            for s in (-1, 0, 1):
                slot(s, s % 2)
            with eng.Fori(0, (NB - 4) // 2) as i:
                for par in range(2):
                    slot(eng.snap(2 * i + (2 + par)), par)
            for s in (NB - 2, NB - 1):
                slot(s, s % 2)

        def ahead(s):
            return NB - 1 - s if isinstance(s, int) else 2

        def is_slot(s, *which):
            return isinstance(s, int) and s in which

        def tiles_before(b):
            return 0 if is_slot(b, 0, 1) else NT if is_slot(b, NB - 1) else NT // 2

        def steps_before_y(s, t):
            if not is_slot(s, 0, 1):
                return 1
            return 0 if t < (4 if is_slot(s, 0) else 2) else 2

        def x_tile(b, o, lo=0, hi=N):
            if isinstance(b, int):
                return x_sb[:, b % XS, o, lo:hi]
            return x_sb[:, bass.ds(b, 1), o, lo:hi]

        def x_slot(eng, b):
            return b if isinstance(b, int) else eng.snap(b % XS)

        def h_of(b):
            return h_one if is_slot(b, 1) else h_sb

        def flat(b, ap):
            return ap if isinstance(b, int) else ap.rearrange("p (a n) -> p a n", a=1)

        @block.sync
        def _(sp):
            def load_adj(o):
                sp.dma_start(adj_f[:, o, :], adj[o * P:(o + 1) * P, :]).then_inc(s_adj[o], 16)

            def load_x(b, par, stored, tiles=range(CT)):
                xs = x_slot(sp, b)
                for o in tiles:
                    if not is_slot(b, *range(XS)):
                        sp.wait_ge(x_stored[o], stored)
                    src = x[b, o * P:(o + 1) * P, :] if isinstance(b, int) else \
                        x[bass.ds(b, 1), o * P:(o + 1) * P, :].rearrange("b p n -> p b n")
                    sp.dma_start(x_tile(xs, o), src).then_inc(x_loaded[o][par], 16)

            load_adj(0)
            load_adj(1)
            load_x(0, 0, 0, [0])
            load_adj(2)
            load_adj(3)
            load_x(0, 0, 0, range(1, CT))
            load_x(1, 1, 0)
            sp.wait_ge(s_mv, 1)
            load_x(2, 0, 0)

            def slot(s, par):
                xs = None if is_slot(s, -1) else x_slot(sp, s)
                if ahead(s) >= 2 and not is_slot(s, -1, 0):
                    load_x(s + 2, par, s * 16)
                if ahead(s) >= 1:
                    sp.wait_ge(s_qk, s + 2)
                    sp.dma_start(q_dram.rearrange("(p t) -> p t", t=NT), qk_col[:, 1 - par, 0, :]).then_inc(s_qout, 16)
                    if not is_slot(s, -1):
                        sp.wait_ge(s_att, (s + 1) * NT)
                        sp.nop(nofuse=True)
                    sp.wait_ge(s_qout, (s + 2) * 16)
                    sp.dma_start(rows[:, 0, :], q_dram.rearrange("(a n) -> a n", a=1).broadcast_to([P, N]))\
                      .then_inc(s_qbc, 16)
                    sp.wait_ge(s_ab, s + 2)
                    sp.dma_start(ab_dram.rearrange("j (p t) -> p j t", t=NT), ab_col[:, :, :]).then_inc(s_about, 16)
                    sp.wait_ge(s_about, (s + 2) * 16)
                    sp.dma_start(rows[:, :, :],
                                 ab_dram.rearrange("(a j) n -> a j n", a=1).broadcast_to([P, 2, N]))\
                      .then_inc(s_abbc, 16)
                if not is_slot(s, -1):
                    for o in range(OT):
                        sp.wait_ge(s_added, s * GROUPS + (CT + GROUPS - OT + o + 1))
                        dst = out[s, o * P:(o + 1) * P, :] if isinstance(s, int) else \
                            out[bass.ds(s, 1), o * P:(o + 1) * P, :].rearrange("b p n -> p b n")
                        sp.dma_start(dst, x_tile(xs, o)).then_inc(x_stored[o], 16)

            slots(sp, slot)
            for o in range(OT):
                sp.wait_ge(x_stored[o], 16 * NB)

        @block.gpsimd
        def _(pool):
            nc.gpsimd.memset(ident, 0.0).then_inc(s_ident, 1)
            nc.gpsimd.memset(minus_half[:, :], -0.5)
            nc.gpsimd.memset(minus_one[:, :], -1.0)
            nc.gpsimd.memset(three_halves[:, :], 1.5)
            nc.gpsimd.memset(eps[:, :], EPS).then_inc(s_const, 1)
            pool.wait_ge(s_ident, 1)
            nc.gpsimd.affine_select(out=ident, in_=ident, compare_op=ALU.not_equal, fill=1.0, base=0,
                                    pattern=[[-1, P]], channel_multiplier=1).then_inc(s_ident, 1)
            pool.wait_ge(s_const, 1)

            def inverse_root(b):
                STEPS = 8
                pool.wait_ge(s_mv, b + 1)
                nc.gpsimd.tensor_tensor(var_eps[:, :], mean_var[:, :, 1], eps[:, :], ALU.add).then_inc(s_rs, 1)
                pool.wait_ge(s_rs, b * STEPS + 1)
                nc.gpsimd.tensor_tensor(rs0[:, :], var_eps[:, :], minus_half[:, :], ALU.pow).then_inc(s_rs, 1)
                pool.wait_ge(s_rs, b * STEPS + 2)
                nc.gpsimd.tensor_tensor(rs1[:, :], var_eps[:, :], rs0[:, :], ALU.mult).then_inc(s_rs, 1)
                pool.wait_ge(s_rs, b * STEPS + 3)
                nc.gpsimd.tensor_tensor(rs2[:, :], rs1[:, :], rs0[:, :], ALU.mult).then_inc(s_rs, 1)
                pool.wait_ge(s_rs, b * STEPS + 4)
                nc.gpsimd.tensor_tensor(rs3[:, :], rs2[:, :], minus_half[:, :], ALU.mult).then_inc(s_rs, 1)
                pool.wait_ge(s_rs, b * STEPS + 5)
                nc.gpsimd.tensor_tensor(rs1[:, :], rs3[:, :], three_halves[:, :], ALU.add).then_inc(s_rs, 1)
                pool.wait_ge(s_rs, b * STEPS + 6)
                nc.gpsimd.tensor_tensor(rstd[:, :], rs1[:, :], rs0[:, :], ALU.mult).then_inc(s_rs, 1)
                pool.wait_ge(s_rs, b * STEPS + 7)
                nc.gpsimd.tensor_tensor(rs3[:, :], mean_var[:, :, 0], rstd[:, :], ALU.mult).then_inc(s_rs, 1)
                pool.wait_ge(s_rs, b * STEPS + 8)
                nc.gpsimd.tensor_tensor(shift[:, :], rs3[:, :], minus_one[:, :], ALU.mult).then_inc(s_rstd, 1)

            inverse_root(0)

            def slot(s, par):
                if ahead(s) >= 2:
                    inverse_root(s + 2)

            slots(pool, slot)

        @block.scalar
        def _(act):
            for j, w in enumerate((wq, wk)):
                act.dma_start(qk_all[:, j, :], w.rearrange("(a c) -> a c", a=1).broadcast_to([P, C])).then_inc(s_w, 16)
            for j, w in enumerate((wq, wk)):
                act.dma_start(qk_w[:, j, :], w.rearrange("(t p) -> p t", p=P), allow_slow_non_contiguous=True)\
                   .then_inc(s_w, 16)
            act.dma_start(bias[:, :], bm.rearrange("(t p) -> p t", p=P), allow_slow_non_contiguous=True)\
               .then_inc(s_bias, 16)
            for c in range(CT):
                act.wait_ge(s_wT, CT)
                nc.scalar.activation(w_sb[:, 0, c, 0:O], psO[:, c, :], ACT.Copy).then_inc(s_whi, 1)

            def h_hi(b, o, xs):
                if o == 0:
                    act.wait_ge(s_rstd, b + 1)
                if not is_slot(b, 0, 1):
                    act.wait_ge(s_h, b * CT + (o - 1))
                    nc.scalar.activation(flat(b, xn[:, o % 2, :]), x_tile(xs, o), ACT.Identity,
                                         bias=shift[:, o:o + 1], scale=rstd[:, o:o + 1]).then_inc(s_xn, 1)
                nc.scalar.activation(flat(b, h_of(b)[:, 0, o, :]), x_tile(xs, o), ACT.Relu,
                                     bias=shift[:, o:o + 1], scale=rstd[:, o:o + 1]).then_inc(s_hhi, 1)

            def exps(b, par):
                q = qk_col[:, par, 0, :]
                act.wait_ge(s_z, b * 2 + 2)
                nc.scalar.activation(rows[:, 1, :], rows[:, 0, :], ACT.Exp, bias=qmax[:, 2:3], scale=SLOPE)
                nc.scalar.activation(r_col[:, :], z_col[:, 1, :], ACT.Exp)
                nc.scalar.activation(rows[:, 0, :], rows[:, 0, :], ACT.Exp, bias=qmax[:, 1:2]).then_inc(s_e, 1)
                nc.scalar.activation(e_col[:, 0, :], q, ACT.Exp, bias=qmax[:, 1:2])
                nc.scalar.activation(e_col[:, 1, :], q, ACT.Exp, bias=qmax[:, 2:3], scale=SLOPE).then_inc(s_e, 1)

            def att_a_part(b, par, t):
                if t == 0:
                    act.wait_ge(s_e, b * 2 + 2)
                    act.wait_ge(s_abbc, b * 16 + 16)
                if not (is_slot(b, 0) and t < 2):
                    act.wait_ge(s_af, b * NT + (t - 1))
                nc.scalar.activation(att_a[:, t % 2, :], rows[:, 0, :], ACT.Copy,
                                     scale=e_col[:, 0, t:t + 1]).then_inc(s_a, 1)

            def att_hi(b, par, t):
                act.wait_ge(s_af, b * NT + (t + 1))
                nc.scalar.activation(att_sb[:, par, 0, t, :], att_f[:, t % 2, :], ACT.Copy).then_inc(s_ahi, 1)

            def att_steps(b, par, lo, hi):
                for t in range(lo, hi, 2):
                    for step in (att_a_part, att_hi):
                        for u in (t, t + 1):
                            step(b, par, u)
                            yield

            def y_hi(b, par, t):
                act.wait_ge(s_ydone, b * NT + (t + 1))
                nc.scalar.activation(y_sb[:, par, 0, t, :].rearrange("p (j c) -> p j c", j=2),
                                     psY[:, t % 2, :, 0:WB], ACT.Copy).then_inc(s_yhi, 1)

            def relu(s, g):
                act.wait_ge(s_odone, s * GROUPS + (g + 1))
                nc.scalar.activation(psO[:, g % OB, :], psO[:, g % OB, :], ACT.Relu,
                                     bias=bias[:, g % OT:g % OT + 1],
                                     scale=out_scale[:, g % OT:g % OT + 1]).then_inc(s_relu, 1)

            for o in range(CT):
                h_hi(0, o, 0)
            act.wait_ge(s_bias, 16)

            def slot(s, par):
                if is_slot(s, -1):
                    for t in range(NT):
                        y_hi(0, 0, t)
                        if t == 2:
                            exps(0, 0)
                        if t < CT:
                            h_hi(1, t, 1)
                    return
                steps = att_steps(s, par, tiles_before(s), NT)
                for t in range(NT if ahead(s) >= 1 else 0):
                    for _ in range(steps_before_y(s, t)):
                        next(steps, None)
                    y_hi(s + 1, 1 - par, t)
                for _ in steps:
                    pass
                xs = x_slot(act, s + 2) if ahead(s) >= 2 else None
                if is_slot(s, 1):
                    exps(2, 0)
                    relu(1, 0)
                else:
                    relu(s, 0)
                    if ahead(s) >= 1:
                        exps(s + 1, 1 - par)
                relu(s, 1)
                if ahead(s) >= 2:
                    h_hi(s + 2, 0, xs)
                    h_hi(s + 2, 1, xs)
                relu(s, 2)
                if is_slot(s, 0, 1):
                    relu(s, 3)
                if ahead(s) >= 2:
                    h_hi(s + 2, 2, xs)
                    h_hi(s + 2, 3, xs)
                if not is_slot(s, 0, 1):
                    relu(s, 3)
                relu(s, 4)
                if ahead(s) >= 1:
                    steps = att_steps(s + 1, 1 - par, 0, tiles_before(s + 1))
                    for _ in range(4):
                        next(steps, None)
                    relu(s, 5)
                    for _ in steps:
                        pass
                else:
                    relu(s, 5)
                relu(s, 6)
                relu(s, 7)

            slots(act, slot)

        @block.vector
        def _(dve):
            def layer_stats(b, par, o, xs):
                dve.wait_ge(x_loaded[o][par], b * 8 + (16 - 8 * par))
                for j in range(2):
                    step = nc.vector.bn_stats(stats[:, o, j, :], x_tile(xs, o, j * 512, (j + 1) * 512))
                if o < CT - 1:
                    return
                step.then_inc(s_stats, 1)
                dve.wait_ge(s_stats, b + 1)
                dve.nop(nofuse=True)
                for o in range(CT):
                    step = nc.vector.bn_aggr(mean_var[:, o, :], stats[:, o, :, :].rearrange("p a b -> p (a b)"))
                step.then_inc(s_mv, 1)

            def layer_norm(b, o):
                if o == 0:
                    dve.wait_ge(s_rstd, b + 1)
                if not (b == 0 and o < 2):
                    dve.wait_ge(s_h, b * CT + (o - 1))
                nc.vector.tensor_scalar(xn[:, o % 2, :], x_tile(b, o), mean_var[:, o, 0:1], rstd[:, o:o + 1],
                                        ALU.subtract, ALU.mult).then_inc(s_xn, 1)

            def h_lo(b, o):
                dve.wait_ge(s_xn, b * CT + (o + 1))
                dve.wait_ge(s_hhi, b * CT + (o + 1))
                nc.vector.scalar_tensor_tensor(h_of(b)[:, 1, o, :], xn[:, o % 2, :], 0.0,
                                               h_of(b)[:, 0, o, :], ALU.max, ALU.subtract).then_inc(s_h, 1)

            for o in range(OT):
                dve.wait_ge(s_adj[o], 16)
                nc.vector.reduce_max(amax[:, o:o + 1], adj_f[:, o, :], AX.X, apply_absolute_value=True)
                if o == 2:
                    layer_stats(0, 0, 0, 0)
            dve.wait_ge(s_w, 16 * 4)
            for j in range(2):
                step = nc.vector.reduce_max(amax[:, OT + j:OT + j + 1], qk_all[:, j, :], AX.X,
                                            apply_absolute_value=True)
            step.then_inc(s_prep, 1)
            dve.wait_ge(s_prep, 1)
            nc.vector.tensor_scalar(amax_g, amax, MIN_SCALE, None, ALU.max).then_inc(s_prep, 1)
            dve.wait_ge(s_prep, 2)
            nc.vector.tensor_scalar(pow2.bitcast(u32), amax_g.bitcast(u32), EXPONENT_BITS, None,
                                    ALU.bitwise_and).then_inc(s_prep, 1)
            dve.wait_ge(s_prep, 3)
            nc.vector.reciprocal(inv2, pow2).then_inc(s_prep, 1)
            nc.vector.tensor_scalar(out_scale[:, :], pow2[:, 0:OT], 1.0 / ATT_SCALE, None, ALU.mult)
            nc.vector.tensor_copy(qk_scale[:, :], pow2[:, OT:OT + 2])
            dve.wait_ge(s_prep, 4)
            for o in range(OT):
                nc.vector.tensor_scalar(adj_s[:, o, :], adj_f[:, o, :], inv2[:, o:o + 1], None, ALU.mult)
            for j in range(2):
                step = nc.vector.tensor_scalar(qk_ws[:, j, :], qk_w[:, j, :], inv2[:, OT + j:OT + j + 1], None,
                                               ALU.mult)
            step.then_inc(s_prep, 1)
            dve.wait_ge(s_prep, 5)
            w_vec = [w_sb[:, i, :, O:WC].rearrange("p c j -> p j c") for i in range(2)]
            nc.vector.tensor_copy(w_vec[0], qk_ws).then_inc(s_prep, 1)
            layer_stats(0, 0, 1, 0)
            dve.wait_ge(s_prep, 6)
            nc.vector.tensor_tensor(w_vec[1], qk_ws, w_vec[0], ALU.subtract)
            for o in range(2, CT):
                layer_stats(0, 0, o, 0)
            for c in range(CT):
                dve.wait_ge(s_whi, c + 1)
                nc.vector.tensor_tensor(w_sb[:, 1, c, 0:O], psO[:, c, :], w_sb[:, 0, c, 0:O], ALU.subtract)\
                  .then_inc(s_added, 1)
            for o in (0, 2):
                for step in (layer_norm, h_lo):
                    step(0, o)
                    step(0, o + 1)

            def y_lo(b, par, t):
                dve.wait_ge(s_yhi, b * NT + (t + 1))
                if not is_slot(b, 0):
                    step = nc.vector.tensor_tensor(qk_col[:, par, :, t], psY[:, t % 2, 1, WB - 2:WB],
                                                   qk_scale[:, :], ALU.mult)
                    if t == NT - 1:
                        step.then_inc(s_qk, 1)
                nc.vector.tensor_tensor(y_sb[:, par, 1, t, :].rearrange("p (j c) -> p j c", j=2),
                                        psY[:, t % 2, :, 0:WB],
                                        y_sb[:, par, 0, t, :].rearrange("p (j c) -> p j c", j=2),
                                        ALU.subtract).then_inc(s_y, 1)

            def q_max(b, par):
                dve.wait_ge(s_qbc, b * 16 + 16)
                nc.vector.reduce_max(qmax[:, 0:1], rows[:, 0, :], AX.X).then_inc(s_qmax, 1)
                dve.wait_ge(s_qmax, b + 1)
                nc.vector.tensor_scalar(z_col[:, 0, :], qk_col[:, par, 1, :], qmax[:, 0:1], 1.0 - SLOPE,
                                        ALU.add, ALU.mult).then_inc(s_z, 1)
                nc.vector.tensor_scalar(qmax[:, 1:2], qmax[:, 0:1], -1.0, None, ALU.mult)
                nc.vector.tensor_scalar(qmax[:, 2:3], qmax[:, 0:1], -SLOPE, None, ALU.mult)
                dve.wait_ge(s_z, b * 2 + 1)
                nc.vector.tensor_scalar(z_col[:, 1, :], z_col[:, 0, :], Z_CAP, None, ALU.min).then_inc(s_z, 1)

            def denominator(b, t):
                if t == 0:
                    dve.wait_ge(s_e, b * 2 + 1)
                if not (is_slot(b, 0) and t < 2):
                    dve.wait_ge(s_den, b * NT + (t - 1))
                nc.vector.scalar_tensor_tensor(unused[:, t % 2, :], rows[:, 0, :], r_col[:, t:t + 1],
                                               rows[:, 1, :], ALU.mult, ALU.max,
                                               accum_out=den[:, t:t + 1]).then_inc(s_den, 1)

            def a_and_b(b):
                dve.wait_ge(s_den, b * NT + NT)
                nc.vector.reciprocal(rden[:, :], den[:, :]).then_inc(s_rden, 1)
                dve.wait_ge(s_rden, b + 1)
                nc.vector.tensor_scalar(ab_col[:, 1, :], rden[:, :], ATT_SCALE, None, ALU.mult)
                nc.vector.scalar_tensor_tensor(ab_col[:, 0, :], rden[:, :], ATT_SCALE, r_col[:, :],
                                               ALU.mult, ALU.mult).then_inc(s_ab, 1)

            def att_sum(b, par, t):
                if t == 0:
                    dve.wait_ge(s_e, b * 2 + 2)
                dve.wait_ge(s_a, b * NT + (t + 1))
                if not (is_slot(b, 0) and t < 2):
                    dve.wait_ge(s_att, b * NT + (t - 1))
                nc.vector.scalar_tensor_tensor(att_f[:, t % 2, :], rows[:, 1, :], e_col[:, 1, t:t + 1],
                                               att_a[:, t % 2, :], ALU.mult, ALU.max).then_inc(s_af, 1)

            def att_lo(b, par, t):
                dve.wait_ge(s_ahi, b * NT + (t + 1))
                nc.vector.tensor_tensor(att_sb[:, par, 1, t, :], att_f[:, t % 2, :],
                                        att_sb[:, par, 0, t, :], ALU.subtract).then_inc(s_att, 1)

            def att_steps(b, par, lo, hi):
                for t in range(lo, hi, 2):
                    for step in (att_sum, att_lo):
                        for u in (t, t + 1):
                            step(b, par, u)
                            yield

            def add(s, g, xs):
                half, o = divmod(g, OT)
                dve.wait_ge(s_relu, s * GROUPS + (g + 1))
                xt = x_tile(xs, o, half * MH, (half + 1) * MH)
                nc.vector.tensor_tensor(xt, flat(s, psO[:, g % OB, :]), xt, ALU.add).then_inc(s_added, 1)

            def slot(s, par):
                if is_slot(s, -1):
                    layer_stats(1, 1, 0, 1)
                    layer_stats(1, 1, 1, 1)
                    dve.wait_ge(s_qk0, 1)
                    for j in range(2):
                        step = nc.vector.tensor_scalar(qk_col[:, 0, j, :], psO[:, OB - 1, j:2 * NT:2],
                                                       qk_scale[:, j:j + 1], None, ALU.mult)
                    step.then_inc(s_qk, 1)
                    layer_stats(1, 1, 2, 1)
                    layer_stats(1, 1, 3, 1)
                    for t in range(NT):
                        y_lo(0, 0, t)
                        if t == 2:
                            q_max(0, 0)
                        elif t < 5:
                            step = {0: layer_norm, 1: h_lo, 3: layer_norm, 4: h_lo}[t]
                            for o in range(2):
                                step(1, (t // 3) * 2 + o)
                        else:
                            denominator(0, 2 * (t - 5))
                            denominator(0, 2 * (t - 5) + 1)
                    return
                steps = att_steps(s, par, tiles_before(s), NT)
                for t in range(NT if ahead(s) >= 1 else 0):
                    if is_slot(s, 0):
                        if t == 0:
                            denominator(0, NT - 2)
                            denominator(0, NT - 1)
                            a_and_b(0)
                        elif t < 3:
                            layer_stats(2, 0, 2 * (t - 1), 2)
                            layer_stats(2, 0, 2 * (t - 1) + 1, 2)
                    for _ in range(steps_before_y(s, t)):
                        next(steps, None)
                    y_lo(s + 1, 1 - par, t)
                for _ in steps:
                    pass
                xs = x_slot(dve, s)
                if ahead(s) >= 2 and not is_slot(s, 0):
                    xs2 = x_slot(dve, s + 2)
                    for o in range(CT):
                        layer_stats(s + 2, par, o, xs2)
                early = 4 if is_slot(s, 1) else 0
                if ahead(s) >= 1:
                    q_max(s + 1, 1 - par)
                    for t in range(early):
                        denominator(s + 1, t)
                add(s, 0, xs)
                if ahead(s) >= 1:
                    for t in range(early, NT):
                        denominator(s + 1, t)
                        if t == 3:
                            add(s, 1, xs)
                    a_and_b(s + 1)
                if ahead(s) < 1 or early > 3:
                    add(s, 1, xs)
                add(s, 2, xs)
                if ahead(s) >= 2:
                    h_lo(s + 2, 0)
                    h_lo(s + 2, 1)
                add(s, 3, xs)
                if ahead(s) >= 2:
                    h_lo(s + 2, 2)
                    h_lo(s + 2, 3)
                if ahead(s) >= 1:
                    steps = att_steps(s + 1, 1 - par, 0, tiles_before(s + 1))
                    for g in (4, 5):
                        for _ in range(4):
                            next(steps, None)
                        add(s, g, xs)
                    for _ in steps:
                        pass
                else:
                    add(s, 4, xs)
                    add(s, 5, xs)
                add(s, 6, xs)
                add(s, 7, xs)

            slots(dve, slot)

        @block.tensor
        def _(pe):
            pe.wait_ge(s_ident, 2)
            pe.wait_ge(s_prep, 5)
            for c in range(CT):
                for o in range(OT):
                    step = nc.tensor.transpose(psO[:, c, o * P:(o + 1) * P], adj_s[:, o, c * P:(c + 1) * P], ident)
                step.then_inc(s_wT, 1)
            pe.wait_ge(s_added, CT)

            def y_gemm(b, par):
                for t in range(NT):
                    if not (is_slot(b, 0) and t < 2):
                        pe.wait_ge(s_y, b * NT + (t - 1))
                    for c in range(CT):
                        if t == 0:
                            pe.wait_ge(s_h, b * CT + (c + 1))
                        for n, (hp, wp) in enumerate(((0, 0), (0, 1), (1, 0))):
                            for j in range(2):
                                step = nc.tensor.matmul(psY[:, t % 2, j, 0:WB], h_of(b)[:, hp, c, t:N:NT],
                                                        w_sb[:, wp, c, j * WB:(j + 1) * WB],
                                                        start=(c == 0 and n == 0), stop=(c == CT - 1 and n == 2))
                    step.then_inc(s_ydone, 1)

            def out_part(s, par, g, t):
                half, o = divmod(g, OT)
                if t == 0:
                    pe.wait_ge(s_added, s * GROUPS + (g + 1))
                if g == 0:
                    pe.wait_ge(s_y, s * NT + (t + 1))
                    pe.wait_ge(s_att, s * NT + (t + 1))
                for n, (yp, ap) in enumerate(((0, 0), (0, 1), (1, 0))):
                    step = nc.tensor.matmul(psO[:, g % OB, :], y_sb[:, par, yp, t, o * P:(o + 1) * P],
                                            att_sb[:, par, ap, t, half * MH:(half + 1) * MH],
                                            start=(t == 0 and n == 0), stop=(t == NT - 1 and n == 2))
                if t == NT - 1:
                    step.then_inc(s_odone, 1)

            def out_gemm(s, par):
                making = is_slot(s, 0, 1)
                if making:
                    for t in range(NT):
                        for g in range(OT):
                            out_part(s, par, g, t)
                for g in range(OT if making else 0, GROUPS):
                    for t in range(NT):
                        out_part(s, par, g, t)

            for c in range(CT):
                pe.wait_ge(s_h, c + 1)
            for t in range(NT):
                for c in range(CT):
                    for n, (hp, wp) in enumerate(((0, 0), (0, 1), (1, 0))):
                        step = nc.tensor.matmul(psO[:, OB - 1, 2 * t:2 * t + 2], h_sb[:, hp, c, t:N:NT],
                                                w_sb[:, wp, c, O:WC],
                                                start=(c == 0 and n == 0), stop=(c == CT - 1 and n == 2))
            step.then_inc(s_qk0, 1)

            def slot(s, par):
                if ahead(s) >= 1:
                    y_gemm(s + 1, 1 - par)
                if is_slot(s, 0):
                    pe.wait_ge(s_qk, 1)
                if not is_slot(s, -1):
                    out_gemm(s, par)

            slots(pe, slot)


_INS = ['x', 'adj', 'L0_gnn_wq', 'L0_gnn_wk', 'L0_gnn_bm']


def kernel(**inputs):
    import numpy as _np
    import concourse.bacc as _bacc
    from concourse import mybir as _mybir
    from concourse.bass_utils import run_bass_kernel_spmd as _run

    nc = _bacc.Bacc("TRN2", target_bir_lowering=False, num_devices=1)
    arrays, args = {}, []
    for name in _INS:
        a = _np.ascontiguousarray(inputs[name])
        arrays[f"in_{name}_dram"] = a
        args.append(nc.dram_tensor(f"in_{name}_dram", a.shape, _mybir.dt.from_np(a.dtype), kind="ExternalInput").ap())
    shape = _np.shape(inputs['x'])
    args.append(nc.dram_tensor("out_0_dram", shape, _mybir.dt.float32, kind="ExternalOutput").ap())
    preln_graph_attention_kernel(nc, *args)
    r = _run(nc, [arrays], core_ids=[0])
    return r.results[0]["out_0_dram"]
```
